# Optimizing a Trainium2 kernel written in Bass

```python
import numpy as np
import jax
import jax.numpy as jnp

def _softmax(x, axis=-1):
    return jax.nn.softmax(x, axis=axis)
def _gelu(x):
    return jax.nn.gelu(x, approximate=True)
def _silu(x):
    return jax.nn.silu(x)
def _sigmoid(x):
    return jax.nn.sigmoid(x)
def _layernorm(x, axis=-1, eps=1e-5):
    m = jnp.mean(x, axis=axis, keepdims=True)
    v = jnp.var(x, axis=axis, keepdims=True)
    return (x - m) / jnp.sqrt(v + eps)
def _scatter_add(tgt, idx, src, axis=0):
    return tgt.at[idx].add(src)
def _segment_sum(src, seg, n):
    return jax.ops.segment_sum(src, seg, n)

kernel_name = 'mk_conv_preact_d1_conv_nchw64_3bdc3f'

def setup_inputs(seed: int = 0):
    np.random.seed(seed)
    _w = jnp.asarray
    def _rec_inputs():
        import jax
        import jax.numpy as jnp
        _gk = jax.random.key(seed)
        x = -7.791e-05 + 0.5477 * jax.random.normal(jax.random.fold_in(_gk, 1), (16, 64, 256, 256), jnp.float32)
        return x
    x = _rec_inputs()
    def _L0_conv_setup():
        import jax, jax.numpy as jnp
        import numpy as np
        EPS = 0.001
        key = jax.random.key(seed)
        k1, k2 = jax.random.split(key)
        B, C, W, H = (16, 64, 256, 256)
        x = jax.random.normal(k1, (B, C, W, H), dtype=jnp.float32)
        keep = (jax.random.uniform(k2, (B, W, H)) < 0.3).astype(jnp.float32)
        x = x * keep[:, None, :, :]
        return {'x': x}
    _L0_conv_all = _L0_conv_setup()
    _L0_conv_in = {k: v for k, v in _L0_conv_all.items() if k in ()}
    del _L0_conv_all

    return {
        "x": x,
    }

def reference(x):
    import jax
    import jax.numpy as jnp
    def _L0_conv_ref(x):
        import jax, jax.numpy as jnp
        import numpy as np
        EPS = 0.001
        """Faithful masked batchnorm (training mode, affine=False).

            Original: per-batch nonzero() of channel-sum, pad index lists to the max
            count with zeros (i.e. duplicate location (0,0)), gather [B, Nmax, C],
            compute per-channel mean/var over ALL gathered entries (padding included),
            divide by sqrt(var+eps) (mean NOT subtracted in output), scatter back to
            nonzero locations — padded rows also overwrite location (0,0).
            """
        B, C, W, H = x.shape
        x1 = x.sum(axis=1)
        m = x1 != 0
        mf = m.astype(x.dtype)
        n = mf.sum(axis=(1, 2))
        Nmax = n.max()
        pad = Nmax - n
        total = (B * Nmax).astype(x.dtype)
        x00 = x[:, :, 0, 0]
        sum_c = jnp.einsum('bcwh,bwh->c', x, mf) + jnp.einsum('bc,b->c', x00, pad)
        mean = sum_c / total
        d = x - mean[None, :, None, None]
        var = (jnp.einsum('bcwh,bwh->c', d * d, mf) + jnp.einsum('bc,b->c', (x00 - mean[None, :]) ** 2, pad)) / total
        inv = 1.0 / jnp.sqrt(var + EPS)
        xn = x * inv[None, :, None, None]
        out = jnp.where(m[:, None, :, :], xn, x)
        has_pad = (pad > 0)[:, None]
        out = out.at[:, :, 0, 0].set(jnp.where(has_pad, x00 * inv[None, :], out[:, :, 0, 0]))
        return out

    def _gn(v, G=32, eps=1e-5):
        B_, C_, H_, W_ = v.shape
        g = v.reshape(B_, G, C_ // G, H_, W_)
        m = jnp.mean(g, axis=(2, 3, 4), keepdims=True)
        s = jnp.var(g, axis=(2, 3, 4), keepdims=True)
        return ((g - m) / jnp.sqrt(s + eps)).reshape(v.shape)

    def _ln_c(v, eps=1e-6):
        m = jnp.mean(v, axis=1, keepdims=True)
        s = jnp.var(v, axis=1, keepdims=True)
        return (v - m) / jnp.sqrt(s + eps)

    def _ln_t(v, eps=1e-5):
        m = jnp.mean(v, axis=-1, keepdims=True)
        s = jnp.var(v, axis=-1, keepdims=True)
        return (v - m) / jnp.sqrt(s + eps)

    def _to_tokens(v):
        B_, C_, H_, W_ = v.shape
        return v.reshape(B_, C_, H_ * W_).transpose(0, 2, 1)
    def _from_tokens(t, like):
        B_, C_, H_, W_ = like.shape
        return t.transpose(0, 2, 1).reshape(B_, C_, H_, W_)

    x = x + _L0_conv_ref(_gn(x))
    return x


_drawn_inputs = setup_inputs


def setup_inputs(seed=0):
    import zlib

    import numpy as np

    out = dict(_drawn_inputs(seed))
    spreads = {}
    factors = {}
    for name, (base, spread) in spreads.items():
        noise = np.random.default_rng([zlib.crc32(name.encode()), seed]).standard_normal(out[name].shape)
        drawn = base * np.exp(spread * noise) if base else spread * noise
        out[name] = jnp.asarray(drawn.astype(out[name].dtype))
    for name, factor in factors.items():
        out[name] = (out[name] * factor).astype(out[name].dtype)
    return out
```

```python
from contextlib import ExitStack

import concourse.bass as bass
from concourse import mybir

ALU = mybir.AluOpType
ACT = mybir.ActivationFunctionType
F32 = mybir.dt.float32
BF16 = mybir.dt.bfloat16
I32 = mybir.dt.int32
AX_X = mybir.AxisListType.X

P = 128
GROUPS = 32
GN_EPS = 1e-5
BN_EPS = 1e-3
RING = 8
SPARE = 2
SUB_BLOCKS = 2

G_BUFS = 4


def norm_conv_kernel(nc: bass.Bass, x: bass.AP, out: bass.AP):
    B, C, W, H = x.shape
    HALVES = P // C
    N = W * H // HALVES
    BLOCKS = P // HALVES
    BLK = N // BLOCKS
    CHUNK = N // RING
    SUB = SUB_BLOCKS * BLK
    CHUNK_BLOCKS = CHUNK // BLK
    CHUNK_SUBS = CHUNK // SUB
    IMAGE_SUBS = N // SUB
    HALF_SUBS = IMAGE_SUBS // 2
    GROUP_P = P // GROUPS
    TILES = B * IMAGE_SUBS
    CONSTS = 9
    STORES = [B] * (RING - SPARE) + [B - 1] * SPARE + [1] * SPARE
    STATS = 6
    assert P % C == 0 and IMAGE_SUBS % G_BUFS == 0 and BLK <= 512 and CHUNK_SUBS * RING == IMAGE_SUBS and B >= 4

    x_rows = x.rearrange("b c w h -> b (c w h)").rearrange("b (p n) -> b p n", p=P)
    out_rows = out.rearrange("b c w h -> b (c w h)").rearrange("b (p n) -> b p n", p=P)

    ctx = ExitStack()
    with ctx:
        def sb(name, shape, dt=F32):
            return ctx.enter_context(nc.sbuf_tensor(name, shape, dt))

        def psum(name, shape):
            return ctx.enter_context(nc.psum_tensor(name, shape, F32))

        def sem(name):
            return ctx.enter_context(nc.semaphore(name))

        slots = sb("slots", [P, RING + SPARE, CHUNK])
        g = sb("g", [P, G_BUFS, SUB])
        nonzero = sb("nonzero", [P, B, BLK], BF16)
        stats = sb("stats", [P, RING, CHUNK_BLOCKS * STATS])
        mean_var = sb("mean_var", [P, 2])
        ch_stats = sb("ch_stats", [P, 2, B])
        ch_mean = ch_stats[:, 0, :]
        ch_var = ch_stats[:, 1, :]
        group_mean = sb("group_mean", [P, B])
        group_rstd = sb("group_rstd", [P, B])
        dev = sb("dev", [P, B])
        work_a = sb("work_a", [P, B])
        work_b = sb("work_b", [P, B])
        group_var = sb("group_var", [P, B])
        group_std = sb("group_std", [P, B])
        col = sb("col", [P, 8])
        bn_mean, bn_sum, n_max, bn_var, bn_std, bn_w, bn_inv, inv_total = (col[:, i:i + 1] for i in range(8))
        n_part = sb("n_part", [P, B])
        carrier = sb("carrier", [P, 1])[:, :]
        n_row = sb("n_row", [P, 1])[:, :]
        left_out = sb("left_out", [1, 1], I32)
        parity = sb("parity", [P, HALVES, C])
        band = sb("band", [P, 2 * P])
        group_avg = sb("group_avg", [P, P])
        chan_avg = sb("chan_avg", [P, P])
        ones = sb("ones", [P, P])
        first_x = sb("first_x", [P, B])
        first_g = sb("first_g", [P, B])
        first_m = sb("first_m", [P, B])
        first_out = sb("first_out", [P, B])
        pad = sb("pad", [P, B])
        has_pad = sb("has_pad", [P, B])
        tile_sums = sb("tile_sums", [P, 2])
        tile_acc = sb("tile_acc", [P, 1])[:, :]
        tile_x = slots[:, 0, 0:SUB]
        tile_y = slots[:, 1, 0:SUB]
        tile_c = slots[:, 2, 0:SUB]
        SPREAD_SLOT = 4
        spread = slots[:, SPREAD_SLOT, :].bitcast(BF16)[:, 0:BLOCKS * P] if CHUNK * 2 >= BLOCKS * P else \
            sb("spread", [P, BLOCKS * P], BF16)[:, :]

        pos_sum = [psum(f"pos_sum{i}", [P, BLK]) for i in range(2)]
        small_ps = psum("small_ps", [P, B])
        mask_ps = psum("mask_ps", [P, SUB_BLOCKS, 512])

        consts_ready = sem("consts_ready")
        band_ready = sem("band_ready")
        aggregated = sem("aggregated")
        kept = sem("kept")
        loaded = [sem(f"loaded{s}") for s in range(RING + SPARE)]
        stored = [sem(f"stored{s}") for s in range(RING + SPARE)]
        chunk_summed = sem("chunk_summed")
        dve_step = sem("dve_step")
        small_in = sem("small_in")
        small_out = sem("small_out")
        sqrt_in = sem("sqrt_in")
        sqrt_out = sem("sqrt_out")
        g_ready = sem("g_ready")
        g_summed = sem("g_summed")
        out_ready = sem("out_ready")
        mask_done = sem("mask_done")
        flag_ready = sem("flag_ready")
        spread_ready = sem("spread_ready")
        first_loaded = sem("first_loaded")
        first_mask = sem("first_mask")
        first_done = sem("first_done")
        first_stored = sem("first_stored")
        tile_loaded = sem("tile_loaded")
        tile_mask = sem("tile_mask")
        tile_step = sem("tile_step")
        tile_used = sem("tile_used")
        tile_out = sem("tile_out")
        tile_stored = sem("tile_stored")

        def column_slot(o_is_first, o_is_second, c):
            if o_is_first:
                return c
            if o_is_second:
                return RING + c if c < SPARE else c - SPARE
            return (c - SPARE) % RING

        def columns(c):
            return slice(c * CHUNK, (c + 1) * CHUNK)

        def load(sp, b, c, s):
            sp.dma_start(slots[:, s, :], x_rows[b, :, columns(c)]).then_inc(loaded[s], 16)

        block = ctx.enter_context(nc.Block())

        @block.sync
        def _(sp):
            for c in range(RING):
                load(sp, 0, c, c)
            with sp.Fori(1, B) as b:
                for c in range(RING):
                    sp.wait_ge(chunk_summed, b * RING + (c + 1 - RING))
                    load(sp, b, c, c)
            for c in range(RING):
                s = column_slot(False, True, c)
                if c >= SPARE:
                    sp.wait_ge(stored[s], 16)
                load(sp, 0, c, s)
            with sp.Fori(1, B - 1) as b:
                for c in range(RING):
                    s = column_slot(False, False, c)
                    sp.wait_ge(stored[s], b * 16 + (16 if c >= SPARE else 0))
                    load(sp, b, c, s)
            for s in range(RING + SPARE):
                sp.wait_ge(stored[s], STORES[s] * 16)

            sp.wait_ge(flag_ready, 1)
            any_left_out = sp.value_load(left_out[0:1, 0:1], min_val=0, max_val=B * W * H)
            with sp.If(any_left_out > 0):
                with nc.allow_non_contiguous_dma("the first position of every channel"):
                    sp.dma_start(first_x[:, :], x_rows.rearrange("b p n -> p b n")[:, :, 0]).then_inc(first_loaded, 16)
                for sweep in range(2):
                    with sp.Fori(0, B) as b:
                        with sp.Fori(0, IMAGE_SUBS) as t:
                            sp.wait_ge(tile_used, b * IMAGE_SUBS + t + (sweep * TILES + 1))
                            sp.dma_start(tile_x, x_rows[b, :, bass.ds(t * SUB, SUB)]).then_inc(tile_loaded, 16)
                sp.sem_inc(tile_stored, 16)
                with sp.Fori(0, B) as b:
                    with sp.Fori(0, IMAGE_SUBS) as t:
                        sp.wait_ge(tile_used, b * IMAGE_SUBS + t + (2 * TILES + 1))
                        sp.dma_start(tile_x, x_rows[b, :, bass.ds(t * SUB, SUB)]).then_inc(tile_loaded, 16)
                        sp.wait_ge(tile_out, b * IMAGE_SUBS + t + 1)
                        sp.dma_start(out_rows[b, :, bass.ds(t * SUB, SUB)], tile_y).then_inc(tile_stored, 16)
                sp.wait_ge(tile_stored, (TILES + 1) * 16)
                sp.wait_ge(first_done, 1)
                with nc.allow_non_contiguous_dma("the first position of every channel"):
                    sp.dma_start(out_rows.rearrange("b p n -> p b n")[0:P:HALVES, :, 0],
                                 first_out[0:P:HALVES, :]).then_inc(first_stored, 16)
                sp.wait_ge(first_stored, 16)
            sp.nop()

        @block.gpsimd
        def _(pool):
            pool.memset(ones[:, :], 1.0).then_inc(consts_ready, 1)
            pool.memset(parity[:, :, :], 1.0).then_inc(consts_ready, 1)
            pool.memset(group_avg[:, :], 1.0 / GROUP_P).then_inc(consts_ready, 1)
            pool.memset(chan_avg[:, :], 1.0 / (HALVES * B)).then_inc(consts_ready, 1)
            pool.wait_ge(consts_ready, 4)
            pool.affine_select(out=parity[:, :, :], in_=parity[:, :, :], compare_op=ALU.is_equal, fill=0.0, base=0,
                               pattern=[[-1, HALVES], [-HALVES, C]], channel_multiplier=1).then_inc(consts_ready, 1)

            def keep_blocks(t, width, step):
                v = t.rearrange("p (i j) -> p i j", j=width)
                pool.affine_select(out=v, in_=v, compare_op=ALU.is_ge, fill=0.0, base=0,
                                   pattern=[[-width, v.shape[1]], [0, width]],
                                   channel_multiplier=step).then_inc(consts_ready, 1)

            def keep_blocks_end(t, width, step):
                v = t.rearrange("p (i j) -> p i j", j=width)
                pool.affine_select(out=v, in_=v, compare_op=ALU.is_ge, fill=0.0, base=width - step,
                                   pattern=[[width, v.shape[1]], [0, width]],
                                   channel_multiplier=-step).then_inc(consts_ready, 1)

            keep_blocks(group_avg[:, :], GROUP_P, 1)
            keep_blocks(chan_avg[:, :], HALVES, 1)
            pool.wait_ge(consts_ready, 7)
            keep_blocks_end(group_avg[:, :], GROUP_P, 1)
            keep_blocks_end(chan_avg[:, :], HALVES, 1)

            pool.wait_ge(flag_ready, 1)
            any_left_out = pool.value_load(left_out[0:1, 0:1], min_val=0, max_val=B * W * H)
            with pool.If(any_left_out > 0):
                pool.wait_ge(stored[SPREAD_SLOT], STORES[SPREAD_SLOT] * 16)
                v = spread.rearrange("q (k c h) -> q k c h", c=C, h=HALVES)
                pool.memset(spread, 1.0).then_inc(spread_ready, 1)
                pool.wait_ge(spread_ready, 1)
                pool.affine_select(out=v, in_=v, compare_op=ALU.is_equal, fill=0.0, base=0,
                                   pattern=[[-HALVES, BLOCKS], [0, C], [-1, HALVES]],
                                   channel_multiplier=1).then_inc(spread_ready, 1)
            pool.nop()

        @block.scalar
        def _(act):
            for n in range(2):
                act.wait_ge(sqrt_in, n + 1)
                nc.scalar.activation(*((group_std[:, :], group_var[:, :]), (bn_std, bn_var))[n],
                                     ACT.Sqrt).then_inc(sqrt_out, 1)

            def store(b, o, c, s):
                act.wait_ge(out_ready, o * IMAGE_SUBS + (c + 1) * CHUNK_SUBS)
                act.dma_start(out_rows[b, :, columns(c)], slots[:, s, :]).then_inc(stored[s], 16)

            for c in range(RING):
                store(B - 1, 0, c, column_slot(True, False, c))
            for c in range(RING):
                store(0, 1, c, column_slot(False, True, c))
            with act.Fori(1, B - 1) as b:
                for c in range(RING):
                    store(b, b + 1, c, column_slot(False, False, c))

            act.wait_ge(flag_ready, 1)
            any_left_out = act.value_load(left_out[0:1, 0:1], min_val=0, max_val=B * W * H)
            with act.If(any_left_out > 0):
                act.wait_ge(sqrt_in, 3)
                nc.scalar.activation(bn_std, bn_var, ACT.Sqrt).then_inc(sqrt_out, 1)
            act.nop()

        @block.tensor
        def _(pe):
            def small(n, lhsT, rhs, width):
                pe.wait_ge(small_in, n)
                nc.tensor.matmul(small_ps[:, 0:width], lhsT, rhs, start=True, stop=True).then_inc(small_out, 1)

            pe.wait_ge(consts_ready, CONSTS)
            small(1, group_avg[:, :], ch_mean, B)
            small(2, group_avg[:, :], work_b[:, :], B)
            small(3, chan_avg[:, :], bn_sum, 1)
            small(4, chan_avg[:, :], bn_sum, 1)

            def sum_image(o, first):
                for s in range(IMAGE_SUBS):
                    half = s // HALF_SUBS
                    if s % HALF_SUBS == 0 and not first:
                        pe.wait_ge(mask_done, o * 2 + (half - 1))
                    pe.wait_ge(g_ready, o * IMAGE_SUBS + (s + 1))
                    for j in range(SUB_BLOCKS):
                        k = s * SUB_BLOCKS + j
                        last = nc.tensor.matmul(pos_sum[half][:, :], band[:, P - HALVES * k:2 * P - HALVES * k],
                                                g[:, s % G_BUFS, j * BLK:(j + 1) * BLK],
                                                start=(s % HALF_SUBS == 0 and j == 0),
                                                stop=(s % HALF_SUBS == HALF_SUBS - 1 and j == SUB_BLOCKS - 1))
                    last.then_inc(g_summed, 1)

            pe.wait_ge(band_ready, 2)
            sum_image(0, True)
            with pe.Fori(1, B) as o:
                sum_image(o, False)
            small(5, ones[:, :], n_row, 1)

            pe.wait_ge(flag_ready, 1)
            any_left_out = pe.value_load(left_out[0:1, 0:1], min_val=0, max_val=B * W * H)
            with pe.If(any_left_out > 0):
                pe.wait_ge(spread_ready, 2)
                nc.tensor.matmul(mask_ps[:, 0, 0:B], spread[:, 0:P], nonzero[:, :, 0],
                                 start=True, stop=True).then_inc(first_mask, 1)
                small(6, ones[:, :], n_part[:, :], B)
                for sweep in range(3):
                    with pe.Fori(0, B) as b:
                        with pe.Fori(0, IMAGE_SUBS) as t:
                            pe.wait_ge(tile_used, b * IMAGE_SUBS + t + (sweep * TILES + 1))
                            for j in range(SUB_BLOCKS):
                                last = nc.tensor.matmul(mask_ps[:, j, 0:BLK],
                                                        spread[:, bass.ds(t * (SUB_BLOCKS * P) + j * P, P)],
                                                        nonzero[:, b, :], start=True, stop=True)
                            last.then_inc(tile_mask, 1)
                    if sweep < 2:
                        small(7 + sweep, chan_avg[:, :], bn_sum, 1)
            pe.nop()

        def general_vector(dve, link, small, rsqrt):
            even = band[:, P:P + 1]
            dve.wait_ge(first_mask, 1)
            link(nc.vector.tensor_copy(first_m[:, :], mask_ps[:, 0, 0:B]))
            small(6)
            link(nc.vector.tensor_reduce(n_max, small_ps[:, :], AX_X, ALU.max))
            link(nc.vector.tensor_scalar(pad[:, :], small_ps[:, :], -1.0, n_max, ALU.mult, ALU.add))
            link(nc.vector.tensor_scalar(has_pad[:, :], pad[:, :], 0.0, None, ALU.is_gt))
            link(nc.vector.tensor_scalar(pad[:, :], pad[:, :], even, None, ALU.mult))
            link(nc.vector.tensor_scalar(inv_total, n_max, float(B), 1.0, ALU.mult, ALU.max))
            link(nc.vector.reciprocal(inv_total, inv_total))
            dve.wait_ge(first_loaded, 16)
            link(nc.vector.tensor_tensor(first_g[:, :], first_x[:, :], group_mean[:, :], ALU.subtract))
            link(nc.vector.tensor_tensor(first_g[:, :], first_g[:, :], group_rstd[:, :], ALU.mult))

            ops = [0]

            def sweep(n, tile_steps, done):
                with dve.Fori(0, B) as b:
                    with dve.Fori(0, IMAGE_SUBS) as t:
                        i = dve.snap(b * IMAGE_SUBS + t)
                        dve.wait_ge(tile_loaded, i * 16 + (n * TILES + 1) * 16)
                        dve.wait_ge(tile_mask, i + (n * TILES + 1))
                        if n == 2:
                            dve.wait_ge(tile_stored, (i + 1) * 16)
                        todo = tile_steps(b)
                        for k, step in enumerate(todo):
                            step().then_inc(tile_step, 1)
                            dve.wait_ge(tile_step, i * len(todo) + (ops[0] + k + 1))
                        for s in done:
                            dve.sem_inc(s, 1)
                ops[0] += TILES * len(todo)

            x_t = tile_x.rearrange("p (k j) -> p k j", k=SUB_BLOCKS)
            a_t, b_t, c_t, y_t = (v.rearrange("p (k j) -> p k j", k=SUB_BLOCKS)
                                  for v in (g[:, 0, :], g[:, 1, :], tile_c, tile_y))
            m_t = mask_ps[:, :, 0:BLK]
            V = nc.vector

            def g_of(b):
                return lambda: V.tensor_scalar(a_t, x_t, group_mean[:, bass.ds(b, 1)], group_rstd[:, bass.ds(b, 1)],
                                               ALU.subtract, ALU.mult)

            link(V.memset(tile_sums[:, :], 0.0))
            dve.sem_inc(tile_used, 1)
            sweep(0, lambda b: [
                g_of(b),
                lambda: V.scalar_tensor_tensor(out=b_t, in0=a_t, scalar=1.0, in1=m_t, op0=ALU.mult, op1=ALU.mult,
                                               accum_out=tile_acc),
                lambda: V.tensor_tensor(tile_sums[:, 0:1], tile_sums[:, 0:1], tile_acc, ALU.add),
            ], [tile_used])
            link(V.tensor_tensor(work_a[:, :], pad[:, :], first_g[:, :], ALU.mult))
            link(V.tensor_reduce(bn_w, work_a[:, :], AX_X, ALU.add))
            link(V.tensor_tensor(bn_sum, bn_w, tile_sums[:, 0:1], ALU.add))
            small(7)
            link(V.tensor_scalar(bn_mean, small_ps[:, 0:1], float(HALVES * B), inv_total, ALU.mult, ALU.mult))

            sweep(1, lambda b: [
                g_of(b),
                lambda: V.tensor_scalar(b_t, a_t, bn_mean, None, ALU.subtract),
                lambda: V.tensor_tensor(a_t, b_t, m_t, ALU.mult),
                lambda: V.scalar_tensor_tensor(out=b_t, in0=a_t, scalar=1.0, in1=a_t, op0=ALU.mult, op1=ALU.mult,
                                               accum_out=tile_acc),
                lambda: V.tensor_tensor(tile_sums[:, 1:2], tile_sums[:, 1:2], tile_acc, ALU.add),
            ], [tile_used])
            link(V.tensor_scalar(work_a[:, :], first_g[:, :], bn_mean, None, ALU.subtract))
            link(V.tensor_tensor(work_a[:, :], work_a[:, :], work_a[:, :], ALU.mult))
            link(V.tensor_tensor(work_a[:, :], work_a[:, :], pad[:, :], ALU.mult))
            link(V.tensor_reduce(bn_w, work_a[:, :], AX_X, ALU.add))
            link(V.tensor_tensor(bn_sum, bn_w, tile_sums[:, 1:2], ALU.add))
            small(8)
            link(V.tensor_scalar(bn_var, small_ps[:, 0:1], float(HALVES * B), inv_total, ALU.mult, ALU.mult))
            link(V.tensor_scalar(bn_var, bn_var, BN_EPS, None, ALU.add))
            rsqrt(3, bn_inv, bn_var, bn_std, bn_w)

            link(V.tensor_tensor(first_m[:, :], first_m[:, :], has_pad[:, :], ALU.max))
            link(V.tensor_scalar(work_a[:, :], first_m[:, :], -1.0, 1.0, ALU.mult, ALU.add))
            link(V.scalar_tensor_tensor(out=work_a[:, :], in0=first_m[:, :], scalar=bn_inv, in1=work_a[:, :],
                                        op0=ALU.mult, op1=ALU.add))
            link(V.tensor_tensor(first_g[:, :], first_g[:, :], work_a[:, :], ALU.mult))
            V.tensor_tensor(first_out[:, :], first_g[:, :], first_x[:, :], ALU.add).then_inc(first_done, 1)

            sweep(2, lambda b: [
                g_of(b),
                lambda: V.tensor_scalar(b_t, m_t, -1.0, 1.0, ALU.mult, ALU.add),
                lambda: V.scalar_tensor_tensor(out=c_t, in0=m_t, scalar=bn_inv, in1=b_t, op0=ALU.mult, op1=ALU.add),
                lambda: V.tensor_tensor(b_t, a_t, c_t, ALU.mult),
                lambda: V.tensor_tensor(y_t, b_t, x_t, ALU.add),
            ], [tile_used, tile_out])

        @block.vector
        def _(dve):
            steps = [0]

            def link(ins):
                steps[0] += 1
                ins.then_inc(dve_step, 1)
                dve.wait_ge(dve_step, steps[0])

            nc.vector.memset(band[:, :], 0.0).then_inc(band_ready, 1)
            dve.wait_ge(band_ready, 1)
            dve.wait_ge(consts_ready, CONSTS)
            nc.vector.tensor_reduce(band[:, P:P + HALVES], parity[:, :, :], AX_X, ALU.add).then_inc(band_ready, 1)

            with dve.Fori(0, B) as b:
                for c in range(RING):
                    dve.wait_ge(loaded[c], (b + 1) * 16)
                    for k in range(CHUNK_BLOCKS):
                        last = nc.vector.bn_stats(stats[:, c, k * STATS:(k + 1) * STATS],
                                                  slots[:, c, k * BLK:(k + 1) * BLK])
                    last.then_inc(chunk_summed, 1)
                dve.wait_ge(chunk_summed, (b + 1) * RING)
                nc.vector.memset(carrier, 0.0)
                nc.vector.bn_aggr(mean_var[:, :], stats.rearrange("p c s -> p (c s)")).then_inc(aggregated, 1)
                dve.wait_ge(aggregated, b + 1)
                nc.vector.tensor_copy(ch_stats[:, :, b], mean_var[:, :]).then_inc(kept, 1)
            dve.wait_ge(kept, B)

            def small(n):
                dve.sem_inc(small_in, 1)
                dve.wait_ge(small_out, n)

            def rsqrt(n, out_, var, std, t):
                dve.sem_inc(sqrt_in, 1)
                dve.wait_ge(sqrt_out, n)
                link(nc.vector.reciprocal(out_, std))
                link(nc.vector.tensor_tensor(t, out_, out_, ALU.mult))
                link(nc.vector.tensor_tensor(t, t, var, ALU.mult))
                link(nc.vector.tensor_scalar(t, t, -0.5, 1.5, ALU.mult, ALU.add))
                link(nc.vector.tensor_tensor(out_, out_, t, ALU.mult))

            small(1)
            link(nc.vector.tensor_copy(group_mean[:, :], small_ps[:, :]))
            link(nc.vector.tensor_tensor(dev[:, :], ch_mean, group_mean[:, :], ALU.subtract))
            link(nc.vector.tensor_tensor(work_a[:, :], dev[:, :], dev[:, :], ALU.mult))
            link(nc.vector.tensor_tensor(work_b[:, :], work_a[:, :], ch_var, ALU.add))
            small(2)
            link(nc.vector.tensor_scalar(group_var[:, :], small_ps[:, :], GN_EPS, None, ALU.add))
            rsqrt(1, group_rstd[:, :], group_var[:, :], group_std[:, :], work_a[:, :])
            link(nc.vector.tensor_tensor(dev[:, :], dev[:, :], group_rstd[:, :], ALU.mult))
            link(nc.vector.tensor_reduce(bn_sum, dev[:, :], AX_X, ALU.add))
            small(3)
            link(nc.vector.tensor_copy(bn_mean, small_ps[:, 0:1]))
            link(nc.vector.tensor_scalar(dev[:, :], dev[:, :], bn_mean, None, ALU.subtract))
            link(nc.vector.tensor_tensor(dev[:, :], dev[:, :], dev[:, :], ALU.mult))
            link(nc.vector.tensor_tensor(work_a[:, :], group_rstd[:, :], group_rstd[:, :], ALU.mult))
            link(nc.vector.tensor_tensor(work_a[:, :], work_a[:, :], ch_var, ALU.mult))
            link(nc.vector.tensor_tensor(work_a[:, :], work_a[:, :], dev[:, :], ALU.add))
            link(nc.vector.tensor_reduce(bn_sum, work_a[:, :], AX_X, ALU.add))
            small(4)
            link(nc.vector.tensor_scalar(bn_var, small_ps[:, 0:1], BN_EPS, None, ALU.add))
            rsqrt(2, bn_inv, bn_var, bn_std, bn_w)

            def normalise(b, o, s, slot, loads, first):
                if s % CHUNK_SUBS == 0:
                    dve.wait_ge(loaded[slot], loads * 16)
                if not first or s >= G_BUFS:
                    dve.wait_ge(g_summed, o * IMAGE_SUBS + (s + 1 - G_BUFS))
                    dve.wait_ge(out_ready, o * IMAGE_SUBS + (s + 1 - G_BUFS))
                nc.vector.tensor_scalar(g[:, s % G_BUFS, :], sub_tile(slot, s), group_mean[:, bass.ds(b, 1)],
                                        group_rstd[:, bass.ds(b, 1)], ALU.subtract, ALU.mult).then_inc(g_ready, 1)

            def add_residual(o, s, slot):
                dve.wait_ge(g_ready, o * IMAGE_SUBS + (s + 1))
                nc.vector.scalar_tensor_tensor(out=sub_tile(slot, s), in0=g[:, s % G_BUFS, :], scalar=bn_inv,
                                               in1=sub_tile(slot, s), op0=ALU.mult, op1=ALU.add).then_inc(out_ready, 1)

            def take_mask(b, o, half):
                dve.wait_ge(g_summed, o * IMAGE_SUBS + (half + 1) * HALF_SUBS)
                rows = slice(half * (P // 2), (half + 1) * (P // 2))
                nc.vector.tensor_scalar(nonzero[rows, b, :], pos_sum[half][rows, :], 0.0, 0.0, ALU.not_equal, ALU.add,
                                        accum_out=n_part[rows, bass.ds(b, 1)]).then_inc(mask_done, 1)

            def sub_tile(slot, s):
                h = s % CHUNK_SUBS
                return slots[:, slot, h * SUB:(h + 1) * SUB]

            def image(b, o, b_before, where, loads, slot_before):
                for s in range(IMAGE_SUBS):
                    c = s // CHUNK_SUBS
                    normalise(b, o, s, where(c), loads(c), b_before is None)
                    if s:
                        add_residual(o, s - 1, where((s - 1) // CHUNK_SUBS))
                    elif b_before is not None:
                        add_residual(o - 1, IMAGE_SUBS - 1, slot_before)
                    if s == 2 and b_before is not None:
                        take_mask(b_before, o - 1, 1)
                    if s == HALF_SUBS + 2:
                        take_mask(b, o, 0)

            image(B - 1, 0, None, lambda c: column_slot(True, False, c), lambda c: B, None)
            image(0, 1, B - 1, lambda c: column_slot(False, True, c),
                  lambda c: 1 if c < SPARE else B + 1, column_slot(True, False, RING - 1))
            assert column_slot(False, True, RING - 1) == column_slot(False, False, RING - 1)
            with dve.Fori(1, B - 1) as b:
                image(b, b + 1, b - 1, lambda c: column_slot(False, False, c),
                      lambda c: b + (B + 1 if c >= SPARE else B), column_slot(False, False, RING - 1))
            add_residual(B - 1, IMAGE_SUBS - 1, column_slot(False, False, RING - 1))
            take_mask(B - 2, B - 1, 1)

            dve.wait_ge(mask_done, 2 * B)
            link(nc.vector.tensor_reduce(n_row, n_part[:, :], AX_X, ALU.add))
            small(5)
            nc.vector.tensor_scalar(left_out[0:1, 0:1], small_ps[0:1, 0:1], -1.0, float(B * W * H),
                                    ALU.mult, ALU.add).then_inc(flag_ready, 1)

            dve.wait_ge(flag_ready, 1)
            any_left_out = dve.value_load(left_out[0:1, 0:1], min_val=0, max_val=B * W * H)
            with dve.If(any_left_out > 0):
                general_vector(dve, link, small, rsqrt)
            dve.nop()


def kernel(x):
    import numpy as _np
    import concourse.bacc as _bacc
    from concourse.bass_utils import run_bass_kernel_spmd as _run

    nc = _bacc.Bacc("TRN2", target_bir_lowering=False, num_devices=1)
    a = _np.ascontiguousarray(x)
    x_dram = nc.dram_tensor("in_x_dram", a.shape, mybir.dt.from_np(a.dtype), kind="ExternalInput").ap()
    out_dram = nc.dram_tensor("out_0_dram", a.shape, F32, kind="ExternalOutput").ap()
    norm_conv_kernel(nc, x_dram, out_dram)
    r = _run(nc, [{"in_x_dram": a}], core_ids=[0])
    return r.results[0]["out_0_dram"]
```

```python
from contextlib import ExitStack

import concourse.bass as bass
from concourse import mybir

ALU = mybir.AluOpType
ACT = mybir.ActivationFunctionType
F32 = mybir.dt.float32
BF16 = mybir.dt.bfloat16
U8 = mybir.dt.uint8
I32 = mybir.dt.int32
AX_X = mybir.AxisListType.X

P = 128
GROUPS = 32
GN_EPS = 1e-5
BN_EPS = 1e-3
RING = 16
ACT_CHUNKS = (5, 11)
SPARE = 6
SUB_BLOCKS = 2
G_BUFS = 4
MASK_LAG = 3
LEAD = 2


def norm_conv_kernel(nc: bass.Bass, x: bass.AP, out: bass.AP):
    B, C, W, H = x.shape
    HALVES = P // C
    N = W * H // HALVES
    BLOCKS = P // HALVES
    BLK = N // BLOCKS
    CHUNK = N // RING
    SUB = SUB_BLOCKS * BLK
    CHUNK_BLOCKS = CHUNK // BLK
    CHUNK_SUBS = CHUNK // SUB
    IMAGE_SUBS = N // SUB
    HALF_SUBS = IMAGE_SUBS // 2
    GROUP_P = P // GROUPS
    TILES = B * IMAGE_SUBS
    SUM_STEPS, SQUARE_STEPS, OUT_STEPS = 3, 5, 5
    CONSTS = 11
    LOADS = [B - 1] * SPARE + [B] * (RING - SPARE) + [1] * SPARE
    FIRST_PARTS = [CHUNK_SUBS] + [1] * (RING - 1)
    STORES = [B] * (RING - SPARE) + [B - 1] * SPARE + [1] * SPARE
    STORES[0] += CHUNK_SUBS - 1
    DVE_CHUNKS = [c for c in range(RING) if c not in ACT_CHUNKS]
    STATS = 6
    assert 2 * C == P and IMAGE_SUBS % G_BUFS == 0 and BLK <= 512
    assert CHUNK_SUBS * RING == IMAGE_SUBS and B >= 4 and 2 * SPARE <= RING and LEAD == 2 == CHUNK_SUBS and SPARE < RING

    x_rows = x.rearrange("b c w h -> b (c w h)").rearrange("b (p n) -> b p n", p=P)
    out_rows = out.rearrange("b c w h -> b (c w h)").rearrange("b (p n) -> b p n", p=P)

    ctx = ExitStack()
    with ctx:
        def sb(name, shape, dt=F32):
            return ctx.enter_context(nc.sbuf_tensor(name, shape, dt))

        def psum(name, shape):
            return ctx.enter_context(nc.psum_tensor(name, shape, F32))

        def sem(name):
            return ctx.enter_context(nc.semaphore(name))

        slots = sb("slots", [P, RING + SPARE, CHUNK])
        g = sb("g", [P, G_BUFS, SUB])
        nonzero = sb("nonzero", [P, B, BLK], U8)
        DVE_STATS = len(DVE_CHUNKS) * CHUNK_BLOCKS * STATS
        stats = sb("stats", [P, DVE_STATS + len(ACT_CHUNKS) * 3])
        act_stats = stats[:, DVE_STATS:].rearrange("p (a s) -> p a s", s=3)
        shift = stats[:, 1:2]
        neg_shift = sb("neg_shift", [P, 1])[:, :]
        act_sums = sb("act_sums", [P, 2, len(ACT_CHUNKS)])
        act_sum_sq = sb("act_sum_sq", [P, len(ACT_CHUNKS)])
        act_junk = g.rearrange("p (i u) n -> p i (u n)", i=2)[:, :, 0:CHUNK]
        mean_var = sb("mean_var", [P, 2])
        ch_stats = sb("ch_stats", [P, 2, B])
        ch_mean = ch_stats[:, 0, :]
        ch_var = ch_stats[:, 1, :]
        group_mean = sb("group_mean", [P, B])
        group_rstd = sb("group_rstd", [P, B])
        dev = sb("dev", [P, B])
        work_a = sb("work_a", [P, B])
        work_b = sb("work_b", [P, B])
        group_var = sb("group_var", [P, B])
        group_std = sb("group_std", [P, B])
        col = sb("col", [P, 8])
        bn_mean, bn_sum, n_max, bn_var, bn_std, bn_part, bn_inv, inv_total = (col[:, i:i + 1] for i in range(8))
        n_part = sb("n_part", [P, B])
        carrier = sb("carrier", [P, 1])[:, :]
        n_row = sb("n_row", [P, 1])[:, :]
        left_out = sb("left_out", [1, 1], I32)
        parity = sb("parity", [P, HALVES, C])
        band = sb("band", [P, 2 * P])
        group_avg = sb("group_avg", [P, P])
        chan_avg = sb("chan_avg", [P, P])
        ones = sb("ones", [P, P])
        eps = sb("eps", [P, 2])
        first_x = sb("first_x", [P, B])
        first_g = sb("first_g", [P, B])
        first_m = sb("first_m", [P, B])
        first_out = sb("first_out", [P, B])
        pad = sb("pad", [P, B])
        has_pad = sb("has_pad", [P, B])
        tile_sums = sb("tile_sums", [P, 2])
        tile_acc = sb("tile_acc", [P, 1])[:, :]
        tile_x = slots[:, 0, 0:SUB]
        tile_y = slots[:, 1, 0:SUB]
        tile_c = slots[:, 2, 0:SUB]
        image_mask = slots[:, 3, :].bitcast(BF16)[:, 0:BLK]
        first_mask = sb("first_mask", [P, B], BF16)
        SPREAD_SLOTS = range(4, 4 + -(-BLOCKS * P * 2 // (CHUNK * 4)))
        spread = slots[:, SPREAD_SLOTS[0]:SPREAD_SLOTS[-1] + 1, :].rearrange("p s n -> p (s n)") \
            .bitcast(BF16)[:, 0:BLOCKS * P]

        pos_sum = [psum(f"pos_sum{i}", [P, BLK]) for i in range(2)]
        small_ps = psum("small_ps", [P, B])
        mask_ps = psum("mask_ps", [P, SUB_BLOCKS, 512])

        consts_ready = sem("consts_ready")
        band_ready = sem("band_ready")
        aggregated = sem("aggregated")
        kept = sem("kept")
        loaded = [sem(f"loaded{s}") for s in range(RING + SPARE)]
        stored = [sem(f"stored{s}") for s in range(RING + SPARE)]
        chunk_summed = sem("chunk_summed")
        shift_ready = sem("shift_ready")
        act_summed = sem("act_summed")
        act_squared = sem("act_squared")
        act_taken = sem("act_taken")
        dve_step = sem("dve_step")
        small_in = sem("small_in")
        small_out = sem("small_out")
        sqrt_in = sem("sqrt_in")
        sqrt_out = sem("sqrt_out")
        g_ready = sem("g_ready")
        g_summed = sem("g_summed")
        out_ready = sem("out_ready")
        mask_done = sem("mask_done")
        flag_ready = sem("flag_ready")
        spread_ready = sem("spread_ready")
        first_loaded = sem("first_loaded")
        first_spread = sem("first_spread")
        mask_given = sem("mask_given")
        first_done = sem("first_done")
        first_stored = sem("first_stored")
        tile_loaded = sem("tile_loaded")
        tile_mask = sem("tile_mask")
        tile_step = sem("tile_step")
        tile_used = sem("tile_used")
        tile_out = sem("tile_out")
        tile_stored = sem("tile_stored")

        def kept_slot(c):
            return RING + c if c < SPARE else c

        def first_slot(c):
            return c

        def second_slot(c):
            return RING + c if c < SPARE else c - SPARE

        def later_slot(c):
            return (c - SPARE) % RING

        def columns(c):
            return slice(c * CHUNK, (c + 1) * CHUNK)

        def load(sp, b, c, s):
            sp.dma_start(slots[:, s, :], x_rows[b, :, columns(c)]).then_inc(loaded[s], 16)

        def wait_for_stats(sp, b, c):
            by, mine = (act_summed, ACT_CHUNKS) if c in ACT_CHUNKS else (chunk_summed, DVE_CHUNKS)
            sp.wait_ge(by, b * len(mine) + (mine.index(c) + 1 - len(mine)))

        block = ctx.enter_context(nc.Block())

        @block.sync
        def _(sp):
            for c in range(RING):
                load(sp, 0, c, kept_slot(c))
            for c in range(SPARE):
                load(sp, 1, c, c)
            for c in range(SPARE, RING):
                wait_for_stats(sp, 1, c)
                load(sp, 1, c, c)
            with sp.Fori(2, B) as b:
                for c in range(RING):
                    wait_for_stats(sp, b, c)
                    load(sp, b, c, c)
            for c in range(SPARE, RING):
                s = second_slot(c)
                sp.wait_ge(stored[s], FIRST_PARTS[s] * 16)
                load(sp, 0, c, s)
            with sp.Fori(1, B - 1) as b:
                for c in range(RING):
                    s = later_slot(c)
                    sp.wait_ge(stored[s], b * 16 + (FIRST_PARTS[s] - 1 + (1 if c >= SPARE else 0)) * 16)
                    load(sp, b, c, s)
            for s in range(RING + SPARE):
                sp.wait_ge(stored[s], STORES[s] * 16)

            sp.wait_ge(flag_ready, 1)
            any_left_out = sp.value_load(left_out[0:1, 0:1], min_val=0, max_val=B * W * H)
            with sp.If(any_left_out > 0):
                with nc.allow_non_contiguous_dma("the first position of every channel"):
                    sp.dma_start(first_x[:, :], x_rows.rearrange("b p n -> p b n")[:, :, 0]).then_inc(first_loaded, 16)
                for sweep in range(2):
                    with sp.Fori(0, B) as b:
                        with sp.Fori(0, IMAGE_SUBS) as t:
                            sp.wait_ge(tile_used, b * IMAGE_SUBS + t + (sweep * TILES + 1))
                            sp.dma_start(tile_x, x_rows[b, :, bass.ds(t * SUB, SUB)]).then_inc(tile_loaded, 16)
                sp.sem_inc(tile_stored, 16)
                with sp.Fori(0, B) as b:
                    with sp.Fori(0, IMAGE_SUBS) as t:
                        sp.wait_ge(tile_used, b * IMAGE_SUBS + t + (2 * TILES + 1))
                        sp.dma_start(tile_x, x_rows[b, :, bass.ds(t * SUB, SUB)]).then_inc(tile_loaded, 16)
                        sp.wait_ge(tile_out, b * IMAGE_SUBS + t + 1)
                        sp.dma_start(out_rows[b, :, bass.ds(t * SUB, SUB)], tile_y).then_inc(tile_stored, 16)
                sp.wait_ge(tile_stored, (TILES + 1) * 16)
                sp.wait_ge(first_done, 1)
                with nc.allow_non_contiguous_dma("the first position of every channel"):
                    sp.dma_start(out_rows.rearrange("b p n -> p b n")[0:P:HALVES, :, 0],
                                 first_out[0:P:HALVES, :]).then_inc(first_stored, 16)
                sp.wait_ge(first_stored, 16)
            sp.nop()

        @block.gpsimd
        def _(pool):
            pool.memset(ones[:, :], 1.0).then_inc(consts_ready, 1)
            pool.memset(parity[:, :, :], 1.0).then_inc(consts_ready, 1)
            pool.memset(group_avg[:, :], 1.0 / GROUP_P).then_inc(consts_ready, 1)
            pool.memset(chan_avg[:, :], 1.0 / (HALVES * B)).then_inc(consts_ready, 1)
            pool.memset(eps[:, 0:1], GN_EPS).then_inc(consts_ready, 1)
            pool.memset(eps[:, 1:2], BN_EPS).then_inc(consts_ready, 1)
            pool.wait_ge(consts_ready, 6)
            pool.affine_select(out=parity[:, :, :], in_=parity[:, :, :], compare_op=ALU.is_equal, fill=0.0, base=0,
                               pattern=[[-1, HALVES], [-HALVES, C]], channel_multiplier=1).then_inc(consts_ready, 1)

            for t, width in ((group_avg, GROUP_P), (chan_avg, HALVES)):
                v = t[:, :].rearrange("p (i j) -> p i j", j=width)
                pool.affine_select(out=v, in_=v, compare_op=ALU.is_ge, fill=0.0, base=0,
                                   pattern=[[-width, P // width], [0, width]],
                                   channel_multiplier=1).then_inc(consts_ready, 1)
            pool.wait_ge(consts_ready, CONSTS - 2)
            for t, width in ((group_avg, GROUP_P), (chan_avg, HALVES)):
                v = t[:, :].rearrange("p (i j) -> p i j", j=width)
                pool.affine_select(out=v, in_=v, compare_op=ALU.is_ge, fill=0.0, base=width - 1,
                                   pattern=[[width, P // width], [0, width]],
                                   channel_multiplier=-1).then_inc(consts_ready, 1)

            pool.wait_ge(flag_ready, 1)
            any_left_out = pool.value_load(left_out[0:1, 0:1], min_val=0, max_val=B * W * H)
            with pool.If(any_left_out > 0):
                for s in SPREAD_SLOTS:
                    pool.wait_ge(stored[s], STORES[s] * 16)
                v = spread.rearrange("q (k c h) -> q k c h", c=C, h=HALVES)
                pool.memset(spread, 1.0).then_inc(spread_ready, 1)
                pool.wait_ge(spread_ready, 1)
                pool.affine_select(out=v, in_=v, compare_op=ALU.is_equal, fill=0.0, base=0,
                                   pattern=[[-HALVES, BLOCKS], [0, C], [-1, HALVES]],
                                   channel_multiplier=1).then_inc(spread_ready, 1)
            pool.nop()

        @block.scalar
        def _(act):
            def sum_chunks(b, slot_of, loads_of):
                act.wait_ge(act_taken, b + 1)
                act.wait_ge(shift_ready, b + 1)
                for a, c in enumerate(ACT_CHUNKS):
                    if a:
                        act.wait_ge(act_summed, b * len(ACT_CHUNKS) + a)
                    act.wait_ge(loaded[slot_of(c)], loads_of(c) * 16)
                    for i, func in enumerate((ACT.Identity, ACT.Square)):
                        last = nc.scalar.activation(act_junk[:, i, :], slots[:, slot_of(c), :], func, bias=neg_shift,
                                                    accum_out=act_sums[:, i, a:a + 1])
                    last.then_inc(act_summed, 1)

            sum_chunks(0, kept_slot, lambda c: 1)
            with act.Fori(1, B) as b:
                sum_chunks(b, first_slot, lambda c: b + (0 if c < SPARE else 1))

            act.wait_ge(consts_ready, CONSTS)
            nc.scalar.activation(bn_std, eps[:, 0:1], ACT.Sqrt).then_inc(sqrt_out, 1)
            act.wait_ge(small_out, 2)
            nc.scalar.activation(group_std[:, :], small_ps[:, :], ACT.Sqrt, bias=eps[:, 0:1]).then_inc(sqrt_out, 1)
            act.wait_ge(small_out, 4)
            act.wait_ge(sqrt_out, 1)
            nc.scalar.activation(bn_std, small_ps[:, 0:1], ACT.Sqrt, bias=eps[:, 1:2]).then_inc(sqrt_out, 1)

            def store(b, o, c, s):
                act.wait_ge(out_ready, o * IMAGE_SUBS + (c + 1) * CHUNK_SUBS)
                act.dma_start(out_rows[b, :, columns(c)], slots[:, s, :]).then_inc(stored[s], 16)

            for s in range(CHUNK_SUBS):
                act.wait_ge(out_ready, s + 1)
                act.dma_start(out_rows[B - 1, :, s * SUB:(s + 1) * SUB],
                              slots[:, first_slot(0), s * SUB:(s + 1) * SUB]).then_inc(stored[first_slot(0)], 16)
            for c in range(1, RING):
                store(B - 1, 0, c, first_slot(c))
            for c in range(RING):
                store(0, 1, c, second_slot(c))
            with act.Fori(1, B - 1) as b:
                for c in range(RING):
                    store(b, b + 1, c, later_slot(c))

            act.wait_ge(flag_ready, 1)
            any_left_out = act.value_load(left_out[0:1, 0:1], min_val=0, max_val=B * W * H)
            with act.If(any_left_out > 0):
                act.wait_ge(sqrt_in, 1)
                nc.scalar.activation(bn_std, bn_var, ACT.Sqrt).then_inc(sqrt_out, 1)
            act.nop()

        @block.tensor
        def _(pe):
            def small(n, lhsT, rhs, width):
                pe.wait_ge(small_in, n)
                nc.tensor.matmul(small_ps[:, 0:width], lhsT, rhs, start=True, stop=True).then_inc(small_out, 1)

            pe.wait_ge(consts_ready, CONSTS)
            small(1, group_avg[:, :], ch_mean, B)
            small(2, group_avg[:, :], work_b[:, :], B)
            small(3, chan_avg[:, :], bn_sum, 1)
            small(4, chan_avg[:, :], bn_sum, 1)

            def sum_image(o, first):
                for s in range(IMAGE_SUBS):
                    half = s // HALF_SUBS
                    if s % HALF_SUBS == 0 and not first:
                        pe.wait_ge(mask_done, o * 2 + (half - 1))
                    pe.wait_ge(g_ready, o * IMAGE_SUBS + (s + 1))
                    for j in range(SUB_BLOCKS):
                        k = s * SUB_BLOCKS + j
                        last = nc.tensor.matmul(pos_sum[half][:, :], band[:, P - HALVES * k:2 * P - HALVES * k],
                                                g[:, s % G_BUFS, j * BLK:(j + 1) * BLK],
                                                start=(s % HALF_SUBS == 0 and j == 0),
                                                stop=(s % HALF_SUBS == HALF_SUBS - 1 and j == SUB_BLOCKS - 1))
                    last.then_inc(g_summed, 1)

            pe.wait_ge(band_ready, 2)
            sum_image(0, True)
            with pe.Fori(1, B) as o:
                sum_image(o, False)
            small(5, ones[:, :], n_row, 1)

            pe.wait_ge(flag_ready, 1)
            any_left_out = pe.value_load(left_out[0:1, 0:1], min_val=0, max_val=B * W * H)
            with pe.If(any_left_out > 0):
                pe.wait_ge(spread_ready, 2)
                pe.wait_ge(mask_given, 1)
                nc.tensor.matmul(mask_ps[:, 0, 0:B], spread[:, 0:P], first_mask[:, :],
                                 start=True, stop=True).then_inc(first_spread, 1)
                small(6, ones[:, :], n_part[:, :], B)
                for sweep in range(3):
                    with pe.Fori(0, B) as b:
                        with pe.Fori(0, IMAGE_SUBS) as t:
                            pe.wait_ge(mask_given, b + (sweep * B + 2))
                            pe.wait_ge(tile_used, b * IMAGE_SUBS + t + (sweep * TILES + 1))
                            for j in range(SUB_BLOCKS):
                                last = nc.tensor.matmul(mask_ps[:, j, 0:BLK],
                                                        spread[:, bass.ds(t * (SUB_BLOCKS * P) + j * P, P)],
                                                        image_mask, start=True, stop=True)
                            last.then_inc(tile_mask, 1)
                    if sweep < 2:
                        small(7 + sweep, chan_avg[:, :], bn_sum, 1)
            pe.nop()

        @block.vector
        def _(dve):
            steps = [0]

            def note(ins):
                steps[0] += 1
                ins.then_inc(dve_step, 1)

            def link(ins):
                note(ins)
                dve.wait_ge(dve_step, steps[0])

            def rsqrt_column(out_, half_var, std, t):
                link(nc.vector.reciprocal(out_, std))
                link(nc.vector.tensor_scalar(t, half_var, out_, out_, ALU.mult, ALU.mult))
                link(nc.vector.tensor_scalar(out_, t, 1.5, out_, ALU.add, ALU.mult))

            nc.vector.memset(band[:, :], 0.0).then_inc(band_ready, 1)
            dve.wait_ge(band_ready, 1)
            dve.wait_ge(consts_ready, CONSTS)
            nc.vector.tensor_reduce(band[:, P:P + HALVES], parity[:, :, :], AX_X, ALU.add).then_inc(band_ready, 1)

            nc.vector.memset(act_stats[:, :, 0], float(CHUNK))
            dve.sem_inc(act_taken, 1)
            per_image = len(DVE_CHUNKS)
            def image_stats(b, slot_of, loads_of):
                for i, c in enumerate(DVE_CHUNKS):
                    dve.wait_ge(loaded[slot_of(c)], loads_of(c) * 16)
                    for k in range(i * CHUNK_BLOCKS, (i + 1) * CHUNK_BLOCKS):
                        block_x = slots[:, slot_of(c), k % CHUNK_BLOCKS * BLK:(k % CHUNK_BLOCKS + 1) * BLK]
                        last = nc.vector.bn_stats(stats[:, k * STATS:(k + 1) * STATS], block_x)
                    last.then_inc(chunk_summed, 1)
                    if i == 1:
                        dve.wait_ge(chunk_summed, b * per_image + 1)
                        nc.vector.tensor_scalar(neg_shift, shift, -1.0, None, ALU.mult).then_inc(shift_ready, 1)
                    if i == per_image - 3:
                        dve.wait_ge(act_summed, (b + 1) * len(ACT_CHUNKS))
                        nc.vector.tensor_scalar(act_stats[:, :, 1], act_sums[:, 0, :], 1.0 / CHUNK, shift,
                                                ALU.mult, ALU.add)
                        nc.vector.tensor_tensor(act_sum_sq[:, :], act_sums[:, 0, :], act_sums[:, 0, :],
                                                ALU.mult).then_inc(act_squared, 1)
                    if i == per_image - 2:
                        dve.wait_ge(act_squared, b + 1)
                        nc.vector.scalar_tensor_tensor(out=act_stats[:, :, 2], in0=act_sum_sq[:, :],
                                                       scalar=-1.0 / CHUNK, in1=act_sums[:, 1, :],
                                                       op0=ALU.mult, op1=ALU.add).then_inc(act_taken, 1)
                dve.wait_ge(chunk_summed, (b + 1) * per_image)
                nc.vector.memset(carrier, 0.0)
                nc.vector.bn_aggr(mean_var[:, :], stats[:, :]).then_inc(aggregated, 1)
                dve.wait_ge(aggregated, b + 1)
                nc.vector.tensor_copy(ch_stats[:, :, b], mean_var[:, :]).then_inc(kept, 1)

            image_stats(0, kept_slot, lambda c: 1)
            with dve.Fori(1, B) as b:
                image_stats(b, first_slot, lambda c: b + (0 if c < SPARE else 1))
            dve.wait_ge(kept, B)

            def product_with_sum(out_, a, b, total):
                return nc.vector.scalar_tensor_tensor(out=out_, in0=a, scalar=1.0, in1=b, op0=ALU.mult,
                                                      op1=ALU.mult, accum_out=total)

            def normalise(b, o, s, slot, loads, first):
                if s % CHUNK_SUBS == 0:
                    dve.wait_ge(loaded[slot], loads * 16)
                if not first or s >= G_BUFS:
                    dve.wait_ge(g_summed, o * IMAGE_SUBS + (s + 1 - G_BUFS))
                    dve.wait_ge(out_ready, o * IMAGE_SUBS + (s + 1 - G_BUFS))
                nc.vector.tensor_scalar(g[:, s % G_BUFS, :], sub_tile(slot, s), group_mean[:, bass.ds(b, 1)],
                                        group_rstd[:, bass.ds(b, 1)], ALU.subtract, ALU.mult).then_inc(g_ready, 1)

            def add_residual(o, s, slot):
                dve.wait_ge(g_ready, o * IMAGE_SUBS + (s + 1))
                nc.vector.scalar_tensor_tensor(out=sub_tile(slot, s), in0=g[:, s % G_BUFS, :], scalar=bn_inv,
                                               in1=sub_tile(slot, s), op0=ALU.mult, op1=ALU.add).then_inc(out_ready, 1)

            def take_mask(b, o, half):
                dve.wait_ge(g_summed, o * IMAGE_SUBS + (half + 1) * HALF_SUBS)
                rows = slice(half * (P // 2), (half + 1) * (P // 2))
                nc.vector.tensor_scalar(nonzero[rows, b, :], pos_sum[half][rows, :], 0.0, 0.0, ALU.not_equal, ALU.add,
                                        accum_out=n_part[rows, bass.ds(b, 1)]).then_inc(mask_done, 1)

            def sub_tile(slot, s):
                h = s % CHUNK_SUBS
                return slots[:, slot, h * SUB:(h + 1) * SUB]

            def general():
                V = nc.vector
                even = band[:, P:P + 1]
                V.tensor_copy(first_mask[:, :], nonzero[:, :, 0]).then_inc(mask_given, 1)
                dve.wait_ge(first_spread, 1)
                link(V.tensor_copy(first_m[:, :], mask_ps[:, 0, 0:B]))
                dve.sem_inc(small_in, 1)
                dve.wait_ge(small_out, 6)
                link(V.tensor_reduce(n_max, small_ps[:, :], AX_X, ALU.max))
                link(V.tensor_scalar(pad[:, :], small_ps[:, :], -1.0, n_max, ALU.mult, ALU.add))
                link(V.tensor_scalar(has_pad[:, :], pad[:, :], 0.0, None, ALU.is_gt))
                link(V.tensor_scalar(pad[:, :], pad[:, :], even, None, ALU.mult))
                link(V.tensor_scalar(inv_total, n_max, float(B), 1.0, ALU.mult, ALU.max))
                link(V.reciprocal(inv_total, inv_total))
                dve.wait_ge(first_loaded, 16)
                link(V.tensor_tensor(first_g[:, :], first_x[:, :], group_mean[:, :], ALU.subtract))
                link(V.tensor_tensor(first_g[:, :], first_g[:, :], group_rstd[:, :], ALU.mult))

                x_t, a_t, b_t, c_t, y_t = (v.rearrange("p (k j) -> p k j", k=SUB_BLOCKS)
                                           for v in (tile_x, g[:, 0, :], g[:, 1, :], tile_c, tile_y))
                m_t = mask_ps[:, :, 0:BLK]

                def give_mask(b):
                    V.tensor_copy(image_mask, nonzero[:, b, :]).then_inc(mask_given, 1)

                def tile_g(sweep, b, i):
                    dve.wait_ge(tile_loaded, i * 16 + (sweep * TILES + 1) * 16)
                    dve.wait_ge(tile_mask, i + (sweep * TILES + 1))
                    return V.tensor_scalar(a_t, x_t, group_mean[:, bass.ds(b, 1)], group_rstd[:, bass.ds(b, 1)],
                                           ALU.subtract, ALU.mult)

                def then(k, ins):
                    ins.then_inc(tile_step, 1)
                    dve.wait_ge(tile_step, k)

                link(V.memset(tile_sums[:, :], 0.0))
                dve.sem_inc(tile_used, 1)
                with dve.Fori(0, B) as b:
                    give_mask(b)
                    with dve.Fori(0, IMAGE_SUBS) as t:
                        i = dve.snap(b * IMAGE_SUBS + t)
                        k = i * SUM_STEPS
                        then(k + 1, tile_g(0, b, i))
                        then(k + 2, V.scalar_tensor_tensor(out=b_t, in0=a_t, scalar=1.0, in1=m_t, op0=ALU.mult,
                                                           op1=ALU.mult, accum_out=tile_acc))
                        then(k + 3, V.tensor_tensor(tile_sums[:, 0:1], tile_sums[:, 0:1], tile_acc, ALU.add))
                        dve.sem_inc(tile_used, 1)
                link(V.tensor_tensor(work_a[:, :], pad[:, :], first_g[:, :], ALU.mult))
                link(V.tensor_reduce(bn_part, work_a[:, :], AX_X, ALU.add))
                V.tensor_tensor(bn_sum, bn_part, tile_sums[:, 0:1], ALU.add).then_inc(small_in, 1)
                dve.wait_ge(small_out, 7)
                link(V.tensor_scalar(bn_mean, small_ps[:, 0:1], float(HALVES * B), inv_total, ALU.mult, ALU.mult))

                with dve.Fori(0, B) as b:
                    give_mask(b)
                    with dve.Fori(0, IMAGE_SUBS) as t:
                        i = dve.snap(b * IMAGE_SUBS + t)
                        k = i * SQUARE_STEPS + TILES * SUM_STEPS
                        then(k + 1, tile_g(1, b, i))
                        then(k + 2, V.tensor_scalar(b_t, a_t, bn_mean, None, ALU.subtract))
                        then(k + 3, V.tensor_tensor(a_t, b_t, m_t, ALU.mult))
                        then(k + 4, V.scalar_tensor_tensor(out=b_t, in0=a_t, scalar=1.0, in1=a_t, op0=ALU.mult,
                                                           op1=ALU.mult, accum_out=tile_acc))
                        then(k + 5, V.tensor_tensor(tile_sums[:, 1:2], tile_sums[:, 1:2], tile_acc, ALU.add))
                        dve.sem_inc(tile_used, 1)
                link(V.tensor_scalar(work_a[:, :], first_g[:, :], bn_mean, None, ALU.subtract))
                link(V.tensor_tensor(work_a[:, :], work_a[:, :], work_a[:, :], ALU.mult))
                link(V.tensor_tensor(work_a[:, :], work_a[:, :], pad[:, :], ALU.mult))
                link(V.tensor_reduce(bn_part, work_a[:, :], AX_X, ALU.add))
                V.tensor_tensor(bn_sum, bn_part, tile_sums[:, 1:2], ALU.add).then_inc(small_in, 1)
                dve.wait_ge(small_out, 8)
                link(V.tensor_scalar(bn_var, small_ps[:, 0:1], float(HALVES * B), inv_total, ALU.mult, ALU.mult))
                V.tensor_scalar(bn_var, bn_var, BN_EPS, None, ALU.add).then_inc(sqrt_in, 1)
                dve.wait_ge(sqrt_out, 4)
                link(V.tensor_scalar(bn_var, bn_var, -0.5, None, ALU.mult))
                rsqrt_column(bn_inv, bn_var, bn_std, bn_part)

                link(V.tensor_tensor(first_m[:, :], first_m[:, :], has_pad[:, :], ALU.max))
                link(V.tensor_scalar(work_a[:, :], first_m[:, :], -1.0, 1.0, ALU.mult, ALU.add))
                link(V.scalar_tensor_tensor(out=work_a[:, :], in0=first_m[:, :], scalar=bn_inv, in1=work_a[:, :],
                                            op0=ALU.mult, op1=ALU.add))
                link(V.tensor_tensor(first_g[:, :], first_g[:, :], work_a[:, :], ALU.mult))
                V.tensor_tensor(first_out[:, :], first_g[:, :], first_x[:, :], ALU.add).then_inc(first_done, 1)

                with dve.Fori(0, B) as b:
                    give_mask(b)
                    with dve.Fori(0, IMAGE_SUBS) as t:
                        i = dve.snap(b * IMAGE_SUBS + t)
                        k = i * OUT_STEPS + TILES * (SUM_STEPS + SQUARE_STEPS)
                        then(k + 1, tile_g(2, b, i))
                        then(k + 2, V.tensor_scalar(b_t, m_t, -1.0, 1.0, ALU.mult, ALU.add))
                        then(k + 3, V.scalar_tensor_tensor(out=c_t, in0=m_t, scalar=bn_inv, in1=b_t,
                                                           op0=ALU.mult, op1=ALU.add))
                        then(k + 4, V.tensor_tensor(b_t, a_t, c_t, ALU.mult))
                        dve.wait_ge(tile_stored, (i + 1) * 16)
                        then(k + 5, V.tensor_tensor(y_t, b_t, x_t, ALU.add))
                        dve.sem_inc(tile_used, 1)
                        dve.sem_inc(tile_out, 1)

            dve.sem_inc(small_in, 1)
            dve.wait_ge(small_out, 1)
            note(nc.vector.tensor_copy(group_mean[:, :], small_ps[:, :]))
            link(nc.vector.tensor_tensor(dev[:, :], ch_mean, small_ps[:, :], ALU.subtract))
            link(nc.vector.tensor_tensor(work_a[:, :], dev[:, :], dev[:, :], ALU.mult))
            nc.vector.tensor_tensor(work_b[:, :], work_a[:, :], ch_var, ALU.add).then_inc(small_in, 1)
            dve.wait_ge(sqrt_out, 2)
            note(nc.vector.tensor_scalar(group_var[:, :], small_ps[:, :], GN_EPS, None, ALU.add))
            link(nc.vector.reciprocal(group_rstd[:, :], group_std[:, :]))
            link(nc.vector.scalar_tensor_tensor(out=work_a[:, :], in0=group_rstd[:, :], scalar=-0.5,
                                                in1=group_rstd[:, :], op0=ALU.mult, op1=ALU.mult))
            link(nc.vector.tensor_tensor(work_a[:, :], work_a[:, :], group_var[:, :], ALU.mult))
            link(nc.vector.scalar_tensor_tensor(out=group_rstd[:, :], in0=work_a[:, :], scalar=1.5,
                                                in1=group_rstd[:, :], op0=ALU.add, op1=ALU.mult))
            product_with_sum(dev[:, :], dev[:, :], group_rstd[:, :], bn_sum).then_inc(small_in, 1)
            link(nc.vector.tensor_tensor(work_a[:, :], group_rstd[:, :], group_rstd[:, :], ALU.mult))
            note(product_with_sum(work_a[:, :], work_a[:, :], ch_var, bn_part))
            normalise(B - 1, 0, 0, first_slot(0), LOADS[0], True)
            dve.wait_ge(small_out, 3)
            link(nc.vector.tensor_scalar(dev[:, :], dev[:, :], small_ps[:, 0:1], None, ALU.subtract))
            link(product_with_sum(work_b[:, :], dev[:, :], dev[:, :], bn_sum))
            nc.vector.tensor_tensor(bn_sum, bn_sum, bn_part, ALU.add).then_inc(small_in, 1)
            normalise(B - 1, 0, 1, first_slot(0), LOADS[0], True)
            dve.wait_ge(sqrt_out, 3)
            note(nc.vector.tensor_scalar(bn_var, small_ps[:, 0:1], BN_EPS, -0.5, ALU.add, ALU.mult))
            rsqrt_column(bn_inv, bn_var, bn_std, bn_part)

            def image(b, o, b_before, where, loads, slot_before):
                for s in range(LEAD if b_before is None else 0, IMAGE_SUBS):
                    normalise(b, o, s, where(s // CHUNK_SUBS), loads(s // CHUNK_SUBS), b_before is None)
                    if s >= LEAD:
                        add_residual(o, s - LEAD, where((s - LEAD) // CHUNK_SUBS))
                    else:
                        add_residual(o - 1, IMAGE_SUBS - LEAD + s, slot_before)
                    if s == MASK_LAG and b_before is not None:
                        take_mask(b_before, o - 1, 1)
                    if s == HALF_SUBS + MASK_LAG:
                        take_mask(b, o, 0)

            image(B - 1, 0, None, first_slot, lambda c: LOADS[c], None)
            image(0, 1, B - 1, second_slot,
                  lambda c: 1 if c < SPARE else LOADS[second_slot(c)] + 1, first_slot(RING - 1))
            assert second_slot(RING - 1) == later_slot(RING - 1)
            with dve.Fori(1, B - 1) as b:
                image(b, b + 1, b - 1, later_slot,
                      lambda c: b + (LOADS[later_slot(c)] + (1 if c >= SPARE else 0)), later_slot(RING - 1))
            for s in range(IMAGE_SUBS - LEAD, IMAGE_SUBS):
                add_residual(B - 1, s, later_slot(RING - 1))
            take_mask(B - 2, B - 1, 1)

            dve.wait_ge(mask_done, 2 * B)
            nc.vector.tensor_reduce(n_row, n_part[:, :], AX_X, ALU.add).then_inc(small_in, 1)
            dve.wait_ge(small_out, 5)
            nc.vector.tensor_scalar(left_out[0:1, 0:1], small_ps[0:1, 0:1], -1.0, float(B * W * H),
                                    ALU.mult, ALU.add).then_inc(flag_ready, 1)

            dve.wait_ge(flag_ready, 1)
            any_left_out = dve.value_load(left_out[0:1, 0:1], min_val=0, max_val=B * W * H)
            with dve.If(any_left_out > 0):
                general()
            dve.nop()


def kernel(x):
    import numpy as _np
    import concourse.bacc as _bacc
    from concourse.bass_utils import run_bass_kernel_spmd as _run

    nc = _bacc.Bacc("TRN2", target_bir_lowering=False, num_devices=1)
    a = _np.ascontiguousarray(x)
    x_dram = nc.dram_tensor("in_x_dram", a.shape, mybir.dt.from_np(a.dtype), kind="ExternalInput").ap()
    out_dram = nc.dram_tensor("out_0_dram", a.shape, F32, kind="ExternalOutput").ap()
    norm_conv_kernel(nc, x_dram, out_dram)
    r = _run(nc, [{"in_x_dram": a}], core_ids=[0])
    return r.results[0]["out_0_dram"]
```
